# Optimizing a Trainium2 kernel written in Bass

```python
import numpy as np
import jax
import jax.numpy as jnp

def _softmax(x, axis=-1):
    return jax.nn.softmax(x, axis=axis)

def _gelu(x):
    return jax.nn.gelu(x, approximate=True)

def _silu(x):
    return jax.nn.silu(x)

def _sigmoid(x):
    return jax.nn.sigmoid(x)

def _layernorm(x, axis=-1, eps=1e-05):
    m = jnp.mean(x, axis=axis, keepdims=True)
    v = jnp.var(x, axis=axis, keepdims=True)
    return (x - m) / jnp.sqrt(v + eps)

def _scatter_add(tgt, idx, src, axis=0):
    return tgt.at[idx].add(src)

def _segment_sum(src, seg, n):
    return jax.ops.segment_sum(src, seg, n)
kernel_name = 'mk_gnn_preln_d4_gnn_r8_f8f24a'

def setup_inputs(seed: int=0):
    np.random.seed(seed)
    _w = jnp.asarray

    def _rec_inputs():
        import jax
        import jax.numpy as jnp
        _gk = jax.random.key(seed)
        x = -0.000202 + 1 * jax.random.normal(jax.random.fold_in(_gk, 1), (6250, 64), jnp.float32)
        _s = jax.random.randint(jax.random.fold_in(_gk, 2), (100000,), 0, 6250, jnp.int32)
        _d = jax.random.randint(jax.random.fold_in(_gk, 3), (100000,), 0, 6250, jnp.int32)
        _loop = jnp.arange(6250, dtype=jnp.int32)
        src = jnp.concatenate([_s, _d, _loop])
        dst = jnp.concatenate([_d, _s, _loop])
        _o = jnp.argsort(dst, stable=True)
        src = src[_o]
        dst = dst[_o]
        edge_attr_5 = jax.random.uniform(jax.random.fold_in(_gk, 11), (206250, 5), jnp.float32, 0.0, 1)
        edge_attr_64 = -9.77346e-05 + 0.999888 * jax.random.normal(jax.random.fold_in(_gk, 12), (206250, 64), jnp.float32)
        edge_weight = jax.random.uniform(jax.random.fold_in(_gk, 14), (206250,), jnp.float32, 0.0, 0.999999)
        return (x, src, dst, edge_attr_5, edge_attr_64, edge_weight)
    x, src, dst, edge_attr_5, edge_attr_64, edge_weight = _rec_inputs()

    def _L0_gnn_setup():
        import jax, jax.numpy as jnp
        import numpy as np
        N = 12500
        E = 200000
        D = 64

        def _gcn_conv(x, W, b, src, dst, deg_inv_sqrt, n):
            h = x @ W
            norm = deg_inv_sqrt[src] * deg_inv_sqrt[dst]
            msg = h[src] * norm[:, None]
            out = jax.ops.segment_sum(msg, dst, num_segments=n)
            return out + b
        key = jax.random.key(seed)
        ks = jax.random.split(key, 6)
        x = jax.random.normal(ks[0], (N, D), dtype=jnp.float32)
        edge_index = jax.random.randint(ks[1], (2, E), 0, N, dtype=jnp.int64)
        scale = 1.0 / np.sqrt(D)
        W1 = jax.random.normal(ks[2], (D, D), dtype=jnp.float32) * scale
        W2 = jax.random.normal(ks[3], (D, D), dtype=jnp.float32) * scale
        W3 = jax.random.normal(ks[4], (D, D), dtype=jnp.float32) * scale
        b1 = jnp.zeros((D,), jnp.float32)
        b2 = jnp.zeros((D,), jnp.float32)
        b3 = jnp.zeros((D,), jnp.float32)
        return {'x': x, 'edge_index': edge_index, 'W1': W1, 'b1': b1, 'W2': W2, 'b2': b2, 'W3': W3, 'b3': b3}
    _L0_gnn_all = _L0_gnn_setup()
    _L0_gnn_in = {k: v for k, v in _L0_gnn_all.items() if k in ('W1', 'b1', 'W2', 'b2', 'W3', 'b3')}
    del _L0_gnn_all

    def _L1_gnn_setup():
        import jax, jax.numpy as jnp
        import numpy as np
        N_NODES = 12500
        N_EDGES = 156250
        DIM = 64

        def _gcn_norm(edge_index, num_nodes):
            loop = jnp.arange(num_nodes, dtype=edge_index.dtype)
            row = jnp.concatenate([edge_index[0], loop])
            col = jnp.concatenate([edge_index[1], loop])
            w = jnp.ones(row.shape[0], dtype=jnp.float32)
            deg = jax.ops.segment_sum(w, col, num_segments=num_nodes)
            dinv = jnp.where(deg > 0, jax.lax.rsqrt(deg), 0.0)
            norm = dinv[row] * dinv[col]
            return (row, col, norm)

        def _gcn_conv(h, row, col, norm, W, b, num_nodes):
            h = h @ W
            msg = h[row] * norm[:, None]
            out = jax.ops.segment_sum(msg, col, num_segments=num_nodes)
            return out + b
        key = jax.random.key(seed)
        ks = jax.random.split(key, 7)
        x = jax.random.normal(ks[0], (N_NODES, DIM), dtype=jnp.float32)
        edge_index = jax.random.randint(ks[1], (2, N_EDGES), 0, N_NODES, dtype=jnp.int64)
        edge_weight = jax.random.uniform(ks[2], (N_EDGES,), dtype=jnp.float32)
        s = 1.0 / np.sqrt(DIM)
        W1 = jax.random.uniform(ks[3], (DIM, DIM), dtype=jnp.float32, minval=-s, maxval=s)
        b1 = jnp.zeros((DIM,), dtype=jnp.float32)
        W2 = jax.random.uniform(ks[4], (DIM, DIM), dtype=jnp.float32, minval=-s, maxval=s)
        b2 = jnp.zeros((DIM,), dtype=jnp.float32)
        return {'x': x, 'edge_index': edge_index, 'edge_weight': edge_weight, 'W1': W1, 'b1': b1, 'W2': W2, 'b2': b2}
    _L1_gnn_all = _L1_gnn_setup()
    _L1_gnn_in = {k: v for k, v in _L1_gnn_all.items() if k in ('W1', 'b1', 'W2', 'b2')}
    del _L1_gnn_all

    def _L2_gnn_setup():
        import jax, jax.numpy as jnp
        import numpy as np
        N, M, D = (6250, 100000, 64)

        def _mlp1(x, W, b):
            return jax.nn.silu(x @ W + b)

        def _res(h, W1, b1, W2, b2):
            return h + _mlp1(_mlp1(h, W1, b1), W2, b2)

        def _seg_mean(x, idx, n):
            s = jax.ops.segment_sum(x, idx, num_segments=n)
            c = jax.ops.segment_sum(jnp.ones((idx.shape[0], 1), x.dtype), idx, num_segments=n)
            return s / jnp.maximum(c, 1.0)

        def _propagate(h, edge_attr, edge_index, We, be, Wl):
            x_i = h[edge_index[0]]
            x_j = h[edge_index[1]]
            x_edge = jnp.concatenate([x_i, x_j, edge_attr], axis=-1)
            x_edge = _mlp1(x_edge, We, be)
            x_edge = edge_attr @ Wl * x_edge
            x_p = _seg_mean(x_edge, edge_index[0], h.shape[0])
            return x_p + h
        key = jax.random.key(seed)
        ks = jax.random.split(key, 24)
        s = 1.0 / np.sqrt(D)
        se = 1.0 / np.sqrt(3 * D)

        def w(k, shape, scale):
            return jax.random.normal(k, shape, jnp.float32) * scale
        inp = {'nodes': jax.random.normal(ks[0], (N, D), jnp.float32), 'edge_attr': jax.random.normal(ks[1], (M, D), jnp.float32), 'edge_index': jax.random.randint(ks[2], (2, M), 0, N, dtype=jnp.int32), 'Wh': w(ks[3], (D, D), s), 'bh': jnp.zeros((D,), jnp.float32), 'Wm': w(ks[4], (D, D), s), 'bm': jnp.zeros((D,), jnp.float32), 'We': w(ks[5], (3 * D, D), se), 'be': jnp.zeros((D,), jnp.float32), 'Wl': w(ks[6], (D, D), s), 'r1_W1': w(ks[7], (D, D), s), 'r1_b1': jnp.zeros((D,), jnp.float32), 'r1_W2': w(ks[8], (D, D), s), 'r1_b2': jnp.zeros((D,), jnp.float32), 'r2_W1': w(ks[9], (D, D), s), 'r2_b1': jnp.zeros((D,), jnp.float32), 'r2_W2': w(ks[10], (D, D), s), 'r2_b2': jnp.zeros((D,), jnp.float32), 'r3_W1': w(ks[11], (D, D), s), 'r3_b1': jnp.zeros((D,), jnp.float32), 'r3_W2': w(ks[12], (D, D), s), 'r3_b2': jnp.zeros((D,), jnp.float32)}
        return inp
    _L2_gnn_all = _L2_gnn_setup()
    _L2_gnn_in = {k: v for k, v in _L2_gnn_all.items() if k in ('Wh', 'bh', 'Wm', 'bm', 'We', 'be', 'Wl', 'r1_W1', 'r1_b1', 'r1_W2', 'r1_b2', 'r2_W1', 'r2_b1', 'r2_W2', 'r2_b2', 'r3_W1', 'r3_b1', 'r3_W2', 'r3_b2')}
    del _L2_gnn_all

    def _L3_gnn_setup():
        import jax, jax.numpy as jnp
        import numpy as np
        EMB = 64
        HEADS = 2
        NUM_BOND = 5
        NEG_SLOPE = 0.2
        key = jax.random.key(seed)
        ks = jax.random.split(key, 9)
        N, E = (6250, 100000)
        x = jax.random.normal(ks[0], (N, EMB), dtype=jnp.float32)
        edge_index = jax.random.randint(ks[1], (2, E), 0, N, dtype=jnp.int64)
        edge_attr = jax.random.uniform(ks[2], (E, NUM_BOND), dtype=jnp.float32)
        W_lin = jax.random.normal(ks[3], (EMB, HEADS * EMB), dtype=jnp.float32) / np.sqrt(EMB)
        b_lin = jnp.zeros((HEADS * EMB,), dtype=jnp.float32)
        W_edge = jax.random.normal(ks[4], (NUM_BOND, HEADS * EMB), dtype=jnp.float32) / np.sqrt(NUM_BOND)
        b_edge = jnp.zeros((HEADS * EMB,), dtype=jnp.float32)
        att = jax.random.normal(ks[5], (1, HEADS, 2 * EMB), dtype=jnp.float32) / np.sqrt(2 * EMB)
        bias = jnp.zeros((EMB,), dtype=jnp.float32)
        return {'x': x, 'edge_index': edge_index, 'edge_attr': edge_attr, 'W_lin': W_lin, 'b_lin': b_lin, 'W_edge': W_edge, 'b_edge': b_edge, 'att': att, 'bias': bias}
    _L3_gnn_all = _L3_gnn_setup()
    _L3_gnn_in = {k: v for k, v in _L3_gnn_all.items() if k in ('W_lin', 'b_lin', 'W_edge', 'b_edge', 'att', 'bias')}
    del _L3_gnn_all
    return {'x': x, 'src': src, 'dst': dst, 'edge_attr_5': edge_attr_5, 'edge_attr_64': edge_attr_64, 'edge_weight': edge_weight, 'L0_gnn_W1': _L0_gnn_in['W1'], 'L0_gnn_b1': _L0_gnn_in['b1'], 'L0_gnn_W2': _L0_gnn_in['W2'], 'L0_gnn_b2': _L0_gnn_in['b2'], 'L0_gnn_W3': _L0_gnn_in['W3'], 'L0_gnn_b3': _L0_gnn_in['b3'], 'L1_gnn_W1': _L1_gnn_in['W1'], 'L1_gnn_b1': _L1_gnn_in['b1'], 'L1_gnn_W2': _L1_gnn_in['W2'], 'L1_gnn_b2': _L1_gnn_in['b2'], 'L2_gnn_Wh': _L2_gnn_in['Wh'], 'L2_gnn_bh': _L2_gnn_in['bh'], 'L2_gnn_Wm': _L2_gnn_in['Wm'], 'L2_gnn_bm': _L2_gnn_in['bm'], 'L2_gnn_We': _L2_gnn_in['We'], 'L2_gnn_be': _L2_gnn_in['be'], 'L2_gnn_Wl': _L2_gnn_in['Wl'], 'L2_gnn_r1_W1': _L2_gnn_in['r1_W1'], 'L2_gnn_r1_b1': _L2_gnn_in['r1_b1'], 'L2_gnn_r1_W2': _L2_gnn_in['r1_W2'], 'L2_gnn_r1_b2': _L2_gnn_in['r1_b2'], 'L2_gnn_r2_W1': _L2_gnn_in['r2_W1'], 'L2_gnn_r2_b1': _L2_gnn_in['r2_b1'], 'L2_gnn_r2_W2': _L2_gnn_in['r2_W2'], 'L2_gnn_r2_b2': _L2_gnn_in['r2_b2'], 'L2_gnn_r3_W1': _L2_gnn_in['r3_W1'], 'L2_gnn_r3_b1': _L2_gnn_in['r3_b1'], 'L2_gnn_r3_W2': _L2_gnn_in['r3_W2'], 'L2_gnn_r3_b2': _L2_gnn_in['r3_b2'], 'L3_gnn_W_lin': _L3_gnn_in['W_lin'], 'L3_gnn_b_lin': _L3_gnn_in['b_lin'], 'L3_gnn_W_edge': _L3_gnn_in['W_edge'], 'L3_gnn_b_edge': _L3_gnn_in['b_edge'], 'L3_gnn_att': _L3_gnn_in['att'], 'L3_gnn_bias': _L3_gnn_in['bias']}

def reference(x, src, dst, edge_attr_5, edge_attr_64, edge_weight, L0_gnn_W1, L0_gnn_b1, L0_gnn_W2, L0_gnn_b2, L0_gnn_W3, L0_gnn_b3, L1_gnn_W1, L1_gnn_b1, L1_gnn_W2, L1_gnn_b2, L2_gnn_Wh, L2_gnn_bh, L2_gnn_Wm, L2_gnn_bm, L2_gnn_We, L2_gnn_be, L2_gnn_Wl, L2_gnn_r1_W1, L2_gnn_r1_b1, L2_gnn_r1_W2, L2_gnn_r1_b2, L2_gnn_r2_W1, L2_gnn_r2_b1, L2_gnn_r2_W2, L2_gnn_r2_b2, L2_gnn_r3_W1, L2_gnn_r3_b1, L2_gnn_r3_W2, L2_gnn_r3_b2, L3_gnn_W_lin, L3_gnn_b_lin, L3_gnn_W_edge, L3_gnn_b_edge, L3_gnn_att, L3_gnn_bias):
    import jax
    import jax.numpy as jnp

    def _L0_gnn_ref(x, edge_index, W1, b1, W2, b2, W3, b3):
        import jax, jax.numpy as jnp
        import numpy as np
        N = 12500
        E = 200000
        D = 64

        def _gcn_conv(x, W, b, src, dst, deg_inv_sqrt, n):
            h = x @ W
            norm = deg_inv_sqrt[src] * deg_inv_sqrt[dst]
            msg = h[src] * norm[:, None]
            out = jax.ops.segment_sum(msg, dst, num_segments=n)
            return out + b
        n = x.shape[0]
        loops = jnp.arange(n, dtype=edge_index.dtype)
        src = jnp.concatenate([edge_index[0], loops])
        dst = jnp.concatenate([edge_index[1], loops])
        deg = jax.ops.segment_sum(jnp.ones(src.shape[0], x.dtype), dst, num_segments=n)
        deg_inv_sqrt = jnp.where(deg > 0, jax.lax.rsqrt(jnp.maximum(deg, 1.0)), 0.0)
        h = jax.nn.relu(_gcn_conv(x, W1, b1, src, dst, deg_inv_sqrt, n))
        h = jax.nn.relu(_gcn_conv(h, W2, b2, src, dst, deg_inv_sqrt, n))
        h = _gcn_conv(h, W3, b3, src, dst, deg_inv_sqrt, n)
        return h

    def _L1_gnn_ref(x, edge_index, edge_weight, W1, b1, W2, b2):
        import jax, jax.numpy as jnp
        import numpy as np
        N_NODES = 12500
        N_EDGES = 156250
        DIM = 64

        def _gcn_norm(edge_index, num_nodes):
            loop = jnp.arange(num_nodes, dtype=edge_index.dtype)
            row = jnp.concatenate([edge_index[0], loop])
            col = jnp.concatenate([edge_index[1], loop])
            w = jnp.ones(row.shape[0], dtype=jnp.float32)
            deg = jax.ops.segment_sum(w, col, num_segments=num_nodes)
            dinv = jnp.where(deg > 0, jax.lax.rsqrt(deg), 0.0)
            norm = dinv[row] * dinv[col]
            return (row, col, norm)

        def _gcn_conv(h, row, col, norm, W, b, num_nodes):
            h = h @ W
            msg = h[row] * norm[:, None]
            out = jax.ops.segment_sum(msg, col, num_segments=num_nodes)
            return out + b
        n = x.shape[0]
        row, col, norm = _gcn_norm(edge_index, n)
        h = _gcn_conv(x, row, col, norm, W1, b1, n)
        h = jax.nn.relu(h)
        out = _gcn_conv(h, row, col, norm, W2, b2, n)
        return out

    def _L2_gnn_ref(nodes, edge_attr, edge_index, Wh, bh, Wm, bm, We, be, Wl, r1_W1, r1_b1, r1_W2, r1_b2, r2_W1, r2_b1, r2_W2, r2_b2, r3_W1, r3_b1, r3_W2, r3_b2):
        import jax, jax.numpy as jnp
        import numpy as np
        N, M, D = (6250, 100000, 64)

        def _mlp1(x, W, b):
            return jax.nn.silu(x @ W + b)

        def _res(h, W1, b1, W2, b2):
            return h + _mlp1(_mlp1(h, W1, b1), W2, b2)

        def _seg_mean(x, idx, n):
            s = jax.ops.segment_sum(x, idx, num_segments=n)
            c = jax.ops.segment_sum(jnp.ones((idx.shape[0], 1), x.dtype), idx, num_segments=n)
            return s / jnp.maximum(c, 1.0)

        def _propagate(h, edge_attr, edge_index, We, be, Wl):
            x_i = h[edge_index[0]]
            x_j = h[edge_index[1]]
            x_edge = jnp.concatenate([x_i, x_j, edge_attr], axis=-1)
            x_edge = _mlp1(x_edge, We, be)
            x_edge = edge_attr @ Wl * x_edge
            x_p = _seg_mean(x_edge, edge_index[0], h.shape[0])
            return x_p + h
        res_h = nodes
        h = _mlp1(nodes, Wh, bh)
        h = _propagate(h, edge_attr, edge_index, We, be, Wl)
        h = _res(h, r1_W1, r1_b1, r1_W2, r1_b2)
        h = _mlp1(h, Wm, bm)
        h = h + res_h
        h = _res(h, r2_W1, r2_b1, r2_W2, r2_b2)
        h = _res(h, r3_W1, r3_b1, r3_W2, r3_b2)
        h = _propagate(h, edge_attr, edge_index, We, be, Wl)
        return h

    def _L3_gnn_ref(x, edge_index, edge_attr, W_lin, b_lin, W_edge, b_edge, att, bias):
        import jax, jax.numpy as jnp
        import numpy as np
        EMB = 64
        HEADS = 2
        NUM_BOND = 5
        NEG_SLOPE = 0.2
        N = x.shape[0]
        h = (x @ W_lin + b_lin).reshape(N, HEADS, EMB)
        ee = (edge_attr @ W_edge + b_edge).reshape(-1, HEADS, EMB)
        src = edge_index[0]
        dst = edge_index[1]
        x_i = h[src]
        x_j = h[dst] + ee
        att_i, att_j = (att[..., :EMB], att[..., EMB:])
        alpha = (x_i * att_i).sum(-1) + (x_j * att_j).sum(-1)
        alpha = jnp.where(alpha >= 0, alpha, NEG_SLOPE * alpha)
        amax = jax.ops.segment_max(alpha, src, num_segments=N)
        e = jnp.exp(alpha - amax[src])
        denom = jax.ops.segment_sum(e, src, num_segments=N)
        alpha = e / (denom[src] + 1e-16)
        messages = x_j * alpha[:, :, None]
        out = jax.ops.segment_sum(messages, src, num_segments=N)
        out = out.mean(axis=1) + bias
        return out
    edge_index = jnp.stack([src, dst])
    h = jnp.maximum(_layernorm(x, axis=-1), 0.0)
    x = x + _L0_gnn_ref(h, edge_index, L0_gnn_W1, L0_gnn_b1, L0_gnn_W2, L0_gnn_b2, L0_gnn_W3, L0_gnn_b3)
    h = jnp.maximum(_layernorm(x, axis=-1), 0.0)
    x = x + _L1_gnn_ref(h, edge_index, edge_weight, L1_gnn_W1, L1_gnn_b1, L1_gnn_W2, L1_gnn_b2)
    h = jnp.maximum(_layernorm(x, axis=-1), 0.0)
    x = x + _L2_gnn_ref(h, edge_attr_64, edge_index, L2_gnn_Wh, L2_gnn_bh, L2_gnn_Wm, L2_gnn_bm, L2_gnn_We, L2_gnn_be, L2_gnn_Wl, L2_gnn_r1_W1, L2_gnn_r1_b1, L2_gnn_r1_W2, L2_gnn_r1_b2, L2_gnn_r2_W1, L2_gnn_r2_b1, L2_gnn_r2_W2, L2_gnn_r2_b2, L2_gnn_r3_W1, L2_gnn_r3_b1, L2_gnn_r3_W2, L2_gnn_r3_b2)
    h = jnp.maximum(_layernorm(x, axis=-1), 0.0)
    x = x + _L3_gnn_ref(h, edge_index, edge_attr_5, L3_gnn_W_lin, L3_gnn_b_lin, L3_gnn_W_edge, L3_gnn_b_edge, L3_gnn_att, L3_gnn_bias)
    return x

_drawn_inputs = setup_inputs


def setup_inputs(seed=0):
    import zlib

    import numpy as np

    out = dict(_drawn_inputs(seed))
    spreads = {'L0_gnn_b1': (0.0, 0.271),
     'L0_gnn_b2': (0.0, 0.1),
     'L0_gnn_b3': (0.0, 0.1),
     'L1_gnn_b1': (0.0, 0.275),
     'L1_gnn_b2': (0.0, 0.1),
     'L2_gnn_bh': (0.0, 0.487),
     'L2_gnn_bm': (0.0, 0.282),
     'L2_gnn_be': (0.0, 0.8),
     'L2_gnn_r1_b1': (0.0, 0.744),
     'L2_gnn_r1_b2': (0.0, 0.537),
     'L2_gnn_r2_b1': (0.0, 0.441),
     'L2_gnn_r2_b2': (0.0, 0.303),
     'L2_gnn_r3_b1': (0.0, 0.545),
     'L2_gnn_r3_b2': (0.0, 0.314),
     'L3_gnn_b_lin': (0.0, 0.27),
     'L3_gnn_b_edge': (0.0, 0.1),
     'L3_gnn_bias': (0.0, 0.1)}
    factors = {'edge_attr_5': 2.775}
    for name, (base, spread) in spreads.items():
        noise = np.random.default_rng([zlib.crc32(name.encode()), seed]).standard_normal(out[name].shape)
        drawn = base * np.exp(spread * noise) if base else spread * noise
        out[name] = jnp.asarray(drawn.astype(out[name].dtype))
    for name, factor in factors.items():
        out[name] = (out[name] * factor).astype(out[name].dtype)
    return out
```

```python
from contextlib import ExitStack

import concourse.bass as bass
from concourse import mybir

F32 = mybir.dt.float32
BF16 = mybir.dt.bfloat16
I32 = mybir.dt.int32
ALU = mybir.AluOpType
ACT = mybir.ActivationFunctionType
AX = mybir.AxisListType

P = 128
D = 64
N = 6250
E = 206250
NH = -(-N // P)
NP = NH * P
LAST = N - (NH - 1) * P
U = 8
CE = -(-E // (P * 2 * U)) * 2 * U
EP = CE * P
EI = CE // (2 * U)
PAIR = 2 * P
TMAX = (E + NH * (PAIR - 1)) // P
TT = -(-TMAX // (2 * U)) * 2 * U
TI = TT // (2 * U)
TX = TT + 2 * U
SLOTS = TT * P
PAD_LO = 200.0
RW = 72
RD = 2
NB5 = 5
HEADS = 2
LN_EPS = 1e-5
SLOPE = 0.2
BIG = 1e30
CH = 4
CHUNKS = [(c, min(CH, NH - c)) for c in range(0, NH, CH)]
NCH = len(CHUNKS)
LA = HEADS * D + HEADS * NB5 + HEADS
LAS = 160
TQ = TT // 4
PAIRS = U // 2
HI_BITS = 6
assert NH <= 1 << HI_BITS and PAIRS * HI_BITS <= 24 and TQ <= 512
PW = HEADS * D + 2 * HEADS
TAIL = LA - HEADS * D
TR_L2, TR_MEAN, TR_BACK, TR_ATT, TR_TAIL = 5, 6, 7, 8, 9
EV_PQ, EV_ATT, EV_TAIL = 5, 7, 8


class Chain:

    def __init__(self, eng, sem):
        self.eng, self.sem, self.n, self.base = eng, sem, 0, None

    def __call__(self, ins):
        ins.then_inc(self.sem, 1)
        self.n += 1
        self.eng.wait_ge(self.sem, self.n if self.base is None else self.base + self.n)


def build(nc, a, out):
    ctx = ExitStack()
    with ctx:
        def sb(name, shape, dt=F32):
            return ctx.enter_context(nc.sbuf_tensor(name, shape, dt))

        def sem(name):
            return ctx.enter_context(nc.semaphore(name))

        rec_dst = nc.dram_tensor("rec_dst", (SLOTS, RD), F32).ap()
        rec_src = nc.dram_tensor("rec_src", (SLOTS, RW), F32).ap()
        conv_table = [nc.dram_tensor(f"conv_table{k}", (NP, D), F32).ap() for k in range(5)]
        q_table = [nc.dram_tensor(f"q_table{k}", (NP, D), F32).ap() for k in range(2)]
        aj_table = nc.dram_tensor("aj_table", (NP, HEADS), F32).ap()
        h_table = nc.dram_tensor("h_table", (NP, HEADS * D), F32).ap()

        ident = sb("ident", [P, P])
        ones = sb("ones", [P, P])
        tri = sb("tri", [P, P])
        iota_lo = sb("iota_lo", [P, P])
        iota_hi = sb("iota_hi", [P, NH])
        bcol = sb("bcol", [P, 1])
        not_first = sb("not_first", [P, 1])
        arena = sb("arena", [P, 11 * CE + TT])
        col = lambda n, dt=F32: arena[:, n * CE:(n + 1) * CE].bitcast(dt)
        hi_f = [col(4), col(2)]
        lo_f = [col(5), col(3)]
        key_i = [col(1, I32), col(0, I32)]
        key_f = [col(7), col(6)]
        mask = col(8, I32)
        scan = col(9)
        zeros = col(10)
        pos_f = col(11)
        hi_scratch = arena[0:1, 11 * CE:11 * CE + TT]
        tile_ge = arena[:, 9 * CE:9 * CE + TT]
        pos_i = key_i
        FT = [arena[0:D, n * NP:(n + 1) * NP] for n in range(3)]
        acc_a = arena[:, 0:NH * LA]
        alpha_all = arena[:, NH * LA:NH * LA + TX * HEADS]
        smax = arena[:, NH * LA + TX * HEADS:NH * LA + TX * HEADS + NH * HEADS]
        ai_tab = arena[:, NH * LA + TX * HEADS + NH * HEADS:NH * LA + TX * HEADS + 2 * NH * HEADS]
        aend = NH * LA + TX * HEADS + 2 * NH * HEADS
        proj = arena[:, aend:aend + NH * PW].rearrange("p (h w) -> p h w", w=PW)

        cnt = sb("cnt", [P, NH])
        tiles_i = sb("tiles_i", [P, NH], I32)
        tiles_f = sb("tiles_f", [P, NH])
        tiles_inc = sb("tiles_inc", [P, NH])
        first_tile = sb("first_tile", [P, NH])
        start = sb("start", [P, NH])
        zeros_nh = sb("zeros_nh", [P, NH])
        diag = sb("diag", [P, NH])
        hi_row = [sb(f"hi_row{k}", [1, TT // U], I32) for k in range(2)]
        tab_dst = sb("tab_dst", [P, TX * RD])
        tab_src = sb("tab_src", [P, TX * RD])
        tabs = [t[:].rearrange("p (t r) -> p t r", r=RD) for t in (tab_dst, tab_src)]
        tile_iota = tab_src[:, 0:TT]
        degree = [sb(f"degree{k}", [P, NH]) for k in range(2)]
        hist_sb = sb("hist_sb", [NH, P])
        dinv = sb("dinv", [P, NH])
        mean_w = sb("mean_w", [P, NH])
        x = sb("x", [P, NH, D])
        h = sb("h", [P, NH, D])
        hs = sb("hs", [P, NH, D])
        acc = sb("acc", [P, NH, D])
        stat = sb("stat", [P, NH])
        stat2 = sb("stat2", [P, NH])
        ring_i = sb("ring_i", [P, 2, U], I32)
        gat = sb("gat", [P, 2, U, HEADS * D])
        gat64 = [gat[:, q].rearrange("p u d -> p (u d)")[:, 0:U * D].rearrange("p (u d) -> p u d", u=U)
                 for q in range(2)]
        gat2 = [gat[:, q].rearrange("p u d -> p (u d)")[:, 0:U * HEADS].rearrange("p (u d) -> p u d", u=U)
                for q in range(2)]
        onehot = sb("onehot", [P, 2, U, P])
        onehot_t = sb("onehot_t", [P, U * P])
        attr_t = sb("attr_t", [D, U * P])
        pay = sb("pay", [P, 2, U, RW])
        a5 = sb("a5", [P, 2, U, NB5])
        oh16 = onehot[:].rearrange("p q u l -> p (q u l)").bitcast(BF16)
        bh_hi = oh16[:, 0:2 * U * NH].rearrange("p (q u h) -> p q u h", q=2, u=U)
        bh_lo = oh16[:, 2 * U * P:4 * U * P].rearrange("p (q u l) -> p q u l", q=2, u=U)
        zero_bf = sb("zero_bf", [P, P], BF16)
        hT = attr_t[:].rearrange("d (q n) -> d q n", q=2)
        tail_t = onehot_t[0:TAIL, :].rearrange("d (q n) -> d q n", q=2)
        zed, msg = [gat[:, q].rearrange("p u d -> p (u d)")[:, U * D:2 * U * D].rearrange("p (u d) -> p u d", u=U)
                    for q in range(2)]
        masked = hs[:].rearrange("p h d -> p (h d)")[:, 0:HEADS * U * P].rearrange("p (h u l) -> p h u l", h=HEADS, u=U)
        penalty = acc[:].rearrange("p h d -> p (h d)")[:, 0:U * P].rearrange("p (u l) -> p u l", u=U)
        wrow = acc[:].rearrange("p h d -> p (h d)")[:, U * P:U * P + U * LA].rearrange("p (u w) -> p u w", u=U)
        hs_flat = hs[:].rearrange("p h d -> p (h d)")
        acc_flat = acc[:].rearrange("p h d -> p (h d)")

        bank = [ctx.enter_context(nc.psum_tensor(f"bank{n}", [P, 512], F32)) for n in range(8)]

        w_conv = [sb(f"w_conv{k}", [D, D]) for k in range(5)]
        b_conv = [sb(f"b_conv{k}", [P, D]) for k in range(5)]
        CONVS = ["L0_gnn_W1", "L0_gnn_W2", "L0_gnn_W3", "L1_gnn_W1", "L1_gnn_W2"]
        MLPS = ["h", "r1_1", "r1_2", "m", "r2_1", "r2_2", "r3_1", "r3_2"]
        mlp_name = {"h": ("Wh", "bh"), "m": ("Wm", "bm")}
        for r in "123":
            for s in "12":
                mlp_name[f"r{r}_{s}"] = (f"r{r}_W{s}", f"r{r}_b{s}")
        w_mlp = {m: sb(f"w_{m}", [D, D]) for m in MLPS}
        b_mlp = {m: sb(f"b_{m}", [D, 1]) for m in MLPS}
        w_pq = sb("w_pq", [D, 2 * D])
        w_ew = sb("w_ew", [D, 2 * D])
        be_bc = sb("be_bc", [P, D])
        w_ha = sb("w_ha", [D, PW])
        b_ha = sb("b_ha", [P, PW])
        o5, o6 = 2 * HEADS * D, (2 + NB5) * HEADS * D
        att_bc = hs_flat[:, 0:o5].rearrange("p (h t d) -> p h t d", h=HEADS, t=2)
        we5_bc = hs_flat[:, o5:o6].rearrange("p (k h d) -> p k h d", k=NB5, h=HEADS)
        be5_bc = hs_flat[:, o6:o6 + HEADS * D].rearrange("p (h d) -> p h d", h=HEADS)
        w5 = sb("w5", [P, HEADS, NB5])
        c0 = sb("c0", [P, HEADS])
        w_tail = sb("w_tail", [2 * NB5 + 2, D])
        bias_bc = sb("bias_bc", [P, D])
        prod5 = sb("prod5", [P, U, HEADS, NB5])
        sc5 = sb("sc5", [P, U, HEADS])
        sc6 = sb("sc6", [P, U, HEADS])
        ex = sb("ex", [P, U, HEADS])
        rden = sb("rden", [P, NH, HEADS])
        tmax = sb("tmax", [P, PAIRS, HEADS])

        s_const = sem("s_const")
        s_key = sem("s_key")
        s_x0 = sem("s_x0")
        s_x = sem("s_x")
        s_w = sem("s_w")
        s_passed = sem("s_passed")
        s_fillable = sem("s_fillable")
        s_filled = sem("s_filled")
        v_ch = sem("v_ch")
        v_l = [sem(f"v_l{k}") for k in range(4)]
        p_base = sem("p_base")
        v_base = sem("v_base")
        p_hi = sem("p_hi")
        v_pos = sem("v_pos")
        a_ring = [sem(f"a_ring{k}") for k in range(2)]
        d_scat = [[sem(f"d_scat{k}{q}") for q in range(2)] for k in range(2)]
        d_attr = [sem(f"d_attr{q}") for q in range(2)]
        d_tab = sem("d_tab")
        v_oh = sem("v_oh")
        p_hist = sem("p_hist")
        p_hist_end = sem("p_hist_end")
        v_hist = sem("v_hist")
        p_deg = sem("p_deg")

        dve_ln = sem("dve_ln")
        act_ln = sem("act_ln")
        v_h = sem("v_h")
        n_tr = sem("n_tr")
        n_cp = sem("n_cp")
        n_mm = sem("n_mm")
        n_ev = sem("n_ev")
        d_table = sem("d_table")
        f_mm = sem("f_mm")
        f_act = sem("f_act")
        f_res = sem("f_res")
        NPASS = 9
        e_idx = [sem(f"e_idx{k}") for k in range(NPASS)]
        e_oh = [sem(f"e_oh{k}") for k in range(NPASS)]
        e_out = [sem(f"e_out{k}") for k in range(NPASS)]
        e_add = [sem(f"e_add{k}") for k in range(NPASS)]
        d_gat = [[sem(f"d_gat{k}{q}") for q in range(2)] for k in range(NPASS)]
        e_tr = [sem(f"e_tr{k}") for k in range(4)]
        e_cp = [sem(f"e_cp{k}") for k in range(4)]
        e_mm = [sem(f"e_mm{k}") for k in range(4)]
        e_z = [sem(f"e_z{k}") for k in range(4)]
        e_fn = [sem(f"e_fn{k}") for k in range(4)]
        e_msg = [sem(f"e_msg{k}") for k in range(4)]
        d_pay = [[sem(f"d_pay{k}{q}") for q in range(2)] for k in range(4)]
        e_v = [sem(f"e_v{k}") for k in range(2)]
        d_out = sem("d_out")

        W_LOADS = 2 * len(CONVS) + 2 * len(MLPS) + 14

        def hold(eng, s, value):
            eng.wait_ge(s, value)
            eng.sem_inc(s_passed, 1)

        def run_ahead(eng, ahead, now, after=None):
            def group(i, q, more=True):
                now(i, q)
                if more:
                    ahead(i + q, 1 - q)
                if after:
                    after(i, q)

            ahead(0, 0)
            with eng.Fori(0, TI - 1) as i:
                for q in range(2):
                    group(i, q)
            group(TI - 1, 0)
            group(TI - 1, 1, more=False)

        def buckets(eng, t, i, q):
            word = eng.value_load(hi_row[t][0:1, bass.ds(i * 2 + q, 1)], min_val=0, max_val=(1 << 24) - 1)
            return [nc.s_assert_within((word >> (HI_BITS * p)) & ((1 << HI_BITS) - 1), 0, NH - 1,
                                       skip_runtime_bounds_check_because="the chip packed bucket numbers below NH")
                    for p in range(PAIRS)]

        block = ctx.enter_context(nc.Block())

        def nodes_rows(t):
            return t.rearrange("(h l) d -> l h d", l=P)

        @block.sync
        def _(sp):
            for key, name in ((1, "src"), (0, "dst")):
                sp.dma_start(key_i[key], a[name].rearrange("(p c) -> p c", p=P)).then_inc(s_key, 16)
            sp.wait_ge(s_x0, 1)
            xin = a["x"]
            sp.dma_start(x[:, 0:NH - 1, :], xin[0:(NH - 1) * P, :].rearrange("(h l) d -> l h d", l=P)).then_inc(s_x, 16)
            sp.dma_start(x[0:LAST, NH - 1, :], xin[(NH - 1) * P:N, :]).then_inc(s_x, 16)
            sp.wait_ge(s_fillable, 2)
            sp.dma_start(rec_dst.rearrange("(p t) r -> p (t r)", p=P), tab_dst[:, 0:TT * RD]).then_inc(s_filled, 16)
            sp.dma_start(rec_src.rearrange("(p g u) r -> p g (u r)", p=P, u=U),
                         pay[:, 0].rearrange("p u r -> p (u r)").unsqueeze(1).to_broadcast([P, TT // U, U * RW]))\
                .then_inc(s_filled, 16)
            sp.wait_ge(s_filled, 32)
            at64 = a["edge_attr_64"].rearrange("(p c) d -> p c d", p=P)
            at5 = a["edge_attr_5"].rearrange("(p c) d -> p c d", p=P)

            def load_attr(i, q):
                g = i * (2 * U) + q * U
                sp.dma_start(pay[:, q, :, 8:RW], at64[:, bass.ds(g, U), :]).then_inc(d_attr[q], 16)
                sp.dma_start(a5[:, q], at5[:, bass.ds(g, U), :]).then_inc(d_attr[q], 16)

            for q in range(2):
                load_attr(0, q)
            with sp.Fori(1, EI) as i:
                for q in range(2):
                    sp.wait_ge(d_scat[1][q], i * (16 * U))
                    load_attr(i, q)
            for q in range(2):
                sp.wait_ge(d_scat[0][q], EI * 16 * U)
                sp.wait_ge(d_scat[1][q], EI * 16 * U)
            sp.dma_start(tab_dst[:, 0:TT * RD], rec_dst.rearrange("(p t) r -> p (t r)", p=P)).then_inc(d_tab, 16)
            sp.dma_start(tabs[1][:, 0:TT, :], rec_src.rearrange("(p t) r -> p t r", p=P)[:, :, 0:RD]).then_inc(d_tab, 16)

            def store_table(stage, table, tile):
                sp.wait_ge(n_ev, NCH * (stage + 1))
                sp.dma_start(nodes_rows(table), tile).then_inc(d_table, 16)

            for k in range(5):
                store_table(k, conv_table[k], hs[:])

            rec = rec_src.rearrange("(p t) r -> p t r", p=P)

            def load_pay(k, i, q):
                sp.dma_start(pay[:, q], rec[:, bass.ds(i * (2 * U) + q * U, U), :]).then_inc(d_pay[k][q], 16)

            def load_all_pay(k):
                if k:
                    sp.wait_ge(e_out[4 + k], 2 * TI)
                for q in range(2):
                    load_pay(k, 0, q)
                with sp.Fori(1, TI) as i:
                    for q in range(2):
                        sp.wait_ge(e_out[5 + k], i * 2 + (q - 1))
                        load_pay(k, i, q)

            for k in range(2):
                store_table(EV_PQ + k, q_table[k], acc[:])
                load_all_pay(k)
            sp.wait_ge(n_ev, NCH * (EV_ATT + 1))
            sp.dma_start(nodes_rows(h_table), proj[:, :, 0:HEADS * D]).then_inc(d_table, 16)
            sp.dma_start(nodes_rows(aj_table), proj[:, :, HEADS * D + HEADS:PW]).then_inc(d_table, 16)
            load_all_pay(2)
            load_all_pay(3)
            sp.wait_ge(v_h, 10)
            sp.dma_start(out[0:(NH - 1) * P, :].rearrange("(h l) d -> l h d", l=P), x[:, 0:NH - 1, :]).then_inc(d_out, 16)
            sp.dma_start(out[(NH - 1) * P:N, :], x[0:LAST, NH - 1, :]).then_inc(d_out, 16)
            sp.wait_ge(d_out, 32)

        @block.gpsimd
        def _(pool):
            nc.gpsimd.memset(ident[:], 0.0).then_inc(s_const, 1)
            nc.gpsimd.memset(ones[:], 1.0).then_inc(s_const, 1)
            nc.gpsimd.memset(x[:, NH - 1, :], 0.0).then_inc(s_x0, 1)
            nc.gpsimd.iota(iota_lo[:], [[1, P]], base=0, channel_multiplier=0,
                           allow_small_or_imprecise_dtypes=True).then_inc(s_const, 1)
            nc.gpsimd.iota(iota_hi[:], [[1, NH]], base=0, channel_multiplier=0,
                           allow_small_or_imprecise_dtypes=True).then_inc(s_const, 1)
            nc.gpsimd.iota(tile_iota, [[1, TT]], base=0, channel_multiplier=0,
                           allow_small_or_imprecise_dtypes=True).then_inc(s_const, 1)
            pool.wait_ge(s_const, 5)
            nc.gpsimd.affine_select(out=ident[:], in_=ident[:], compare_op=ALU.not_equal, fill=1.0,
                                    base=0, pattern=[[-1, P]], channel_multiplier=1).then_inc(s_const, 1)
            nc.gpsimd.affine_select(out=tri[:], in_=ones[:], compare_op=ALU.is_gt, fill=0.0,
                                    base=0, pattern=[[1, P]], channel_multiplier=-1).then_inc(s_const, 1)
            pool.wait_ge(s_filled, 32)
            for key, table in ((0, rec_dst), (1, rec_src)):
                with pool.Fori(0, EI) as i:
                    for q in range(2):
                        hold(pool, a_ring[key], i * 2 + (q + 1))
                        for u in range(U):
                            src = gat64[q][:, u, 0:RD] if key == 0 else pay[:, q, u, :]
                            nc.gpsimd.indirect_dma_start(
                                table, bass.IndirectOffsetOnAxis(ring_i[:, q, u:u + 1], 0), src, None,
                                bounds_check=SLOTS - 1, oob_is_err=False).then_inc(d_scat[key][q], 16)
                for q in range(2):
                    pool.wait_ge(d_scat[key][q], EI * 16 * U)

            def gather_pass(k, table, tables_stored, rows):
                pool.wait_ge(d_table, tables_stored)
                with pool.Fori(0, TI) as i:
                    for q in range(2):
                        hold(pool, e_idx[k], i * 2 + (q + 1))
                        for u in range(U):
                            nc.gpsimd.indirect_dma_start(
                                rows[q][:, u, :], None, table,
                                bass.IndirectOffsetOnAxis(ring_i[:, q, u:u + 1], 0)).then_inc(d_gat[k][q], 16)

            for k in range(5):
                gather_pass(k, conv_table[k], 16 * (k + 1), gat64)
            for k in range(2):
                gather_pass(5 + k, q_table[k], 16 * (6 + k), gat64)
            gather_pass(7, aj_table, 16 * 9, gat2)
            gather_pass(8, h_table, 16 * 9, [gat[:, 0], gat[:, 1]])

        @block.scalar
        def _(act):
            def load(dst, src):
                act.dma_start(dst, src).then_inc(s_w, 16)
                loads[0] += 1

            loads = [0]
            row = lambda v: v.rearrange("(o d) -> o d", o=1)
            for k, name in enumerate(CONVS):
                load(w_conv[k][:], a[name])
                load(b_conv[k][:], row(a[name.replace("W", "b")]).to_broadcast([P, D]))
            for m in MLPS:
                wn, bn = mlp_name[m]
                load(w_mlp[m][:], a["L2_gnn_" + wn])
                load(b_mlp[m][:], a["L2_gnn_" + bn].rearrange("(d o) -> d o", o=1))
            load(w_pq[:, 0:D], a["L2_gnn_We"][0:D, :])
            load(w_pq[:, D:2 * D], a["L2_gnn_We"][D:2 * D, :])
            load(w_ew[:, 0:D], a["L2_gnn_We"][2 * D:3 * D, :])
            load(w_ew[:, D:2 * D], a["L2_gnn_Wl"])
            load(be_bc[:], row(a["L2_gnn_be"]).to_broadcast([P, D]))
            load(w_ha[:, 0:HEADS * D], a["L3_gnn_W_lin"])
            load(b_ha[:, 0:HEADS * D], row(a["L3_gnn_b_lin"]).to_broadcast([P, HEADS * D]))
            load(hs_flat[:, 0:o5],
                 a["L3_gnn_att"].rearrange("o h d -> o (h d)").to_broadcast([P, HEADS * 2 * D]))
            load(hs_flat[:, o5:o6],
                 a["L3_gnn_W_edge"].rearrange("(o k) d -> o (k d)", o=1).to_broadcast([P, NB5 * HEADS * D]))
            load(hs_flat[:, o6:o6 + HEADS * D], row(a["L3_gnn_b_edge"]).to_broadcast([P, HEADS * D]))
            for hd in range(HEADS):
                load(w_tail[hd * NB5:(hd + 1) * NB5, :], a["L3_gnn_W_edge"][:, hd * D:(hd + 1) * D])
            load(w_tail[2 * NB5:2 * NB5 + 2, :], a["L3_gnn_b_edge"].rearrange("(h d) -> h d", h=HEADS))
            load(bias_bc[:], row(a["L3_gnn_bias"]).to_broadcast([P, D]))
            assert loads[0] == W_LOADS, loads[0]

            def fill(key, i, q):
                g = i * (2 * U) + q * U
                cols = bass.ds(g, U)
                dst = gat64[q][:, :, :] if key == 0 else pay[:, q]
                act.copy(ring_i[:, q, :], pos_i[key][:, cols])
                act.copy(dst[:, :, 0], key_f[1 - key][:, cols])
                last = act.copy(dst[:, :, 1], lo_f[key][:, cols])
                if key == 1:
                    last = act.copy(pay[:, q, :, 2:2 + NB5], a5[:, q])
                last.then_inc(a_ring[key], 1)

            def fill_all(key):
                act.wait_ge(v_pos, key + 1)
                for q in range(2):
                    if key == 1:
                        act.wait_ge(d_attr[q], 32)
                        act.wait_ge(d_scat[0][q], EI * 16 * U)
                    fill(key, 0, q)
                with act.Fori(1, EI) as i:
                    for q in range(2):
                        if key == 1:
                            hold(act, d_attr[q], i * 32 + 32)
                        hold(act, d_scat[key][q], i * (16 * U))
                        fill(key, i, q)

            def root(n):
                act.wait_ge(dve_ln, n + 1)
                act.activation(stat[:], stat2[:], ACT.Sqrt).then_inc(act_ln, 1)

            def node_copies(tr, ev, dst, rows):
                for c, (_, n) in enumerate(CHUNKS):
                    act.wait_ge(n_tr, NCH * tr + c + 1)
                    if c >= 2:
                        act.wait_ge(n_mm, NCH * ev + c - 1)
                    act.copy(dst[0:rows, c % 2, 0:n * P], bank[c % 2][0:rows, 0:n * P]).then_inc(n_cp, 1)

            fill_all(0)
            root(0)
            root(1)
            node_copies(0, 0, hT, D)
            fill_all(1)
            for k in range(1, 5):
                if k == 3:
                    root(2)
                node_copies(k, k, hT, D)
            root(3)

            act.wait_ge(s_w, 16 * W_LOADS)
            for c, (c0_, n) in enumerate(CHUNKS):
                act.wait_ge(n_tr, NCH * TR_L2 + c + 1)
                act.copy(FT[0][:, c0_ * P:(c0_ + n) * P], bank[c % 2][0:D, 0:n * P]).then_inc(n_cp, 1)

            def layer_act(j, m, dst):
                for c, (c0_, n) in enumerate(CHUNKS):
                    act.wait_ge(f_mm, NCH * j + c + 1)
                    act.activation(dst[:, c0_ * P:(c0_ + n) * P], bank[2 + c % 2][0:D, 0:n * P], ACT.Silu,
                                   bias=b_mlp[m][:, 0:1]).then_inc(f_act, 1)

            def propagate_act(k):
                def copies(i, q):
                    hold(act, e_tr[k], i * 2 + (q + 1))
                    for b in range(2):
                        act.copy(onehot_t[:, b * 512:(b + 1) * 512], bank[b][:])
                        last = act.copy(attr_t[:, b * 512:(b + 1) * 512], bank[2 + b][0:D, :])
                    last.then_inc(e_cp[k], 1)

                def silu(i, q):
                    hold(act, e_z[k], i * 2 + (q + 1))
                    act.activation(msg[:], zed[:], ACT.Silu).then_inc(e_fn[k], 1)

                run_ahead(act, copies, silu)

            layer_act(0, "h", FT[1])
            propagate_act(0)
            layer_act(1, "r1_1", FT[2])
            layer_act(2, "r1_2", FT[2])
            layer_act(3, "m", FT[1])
            layer_act(4, "r2_1", FT[2])
            layer_act(5, "r2_2", FT[2])
            layer_act(6, "r3_1", FT[2])
            layer_act(7, "r3_2", FT[2])
            propagate_act(1)

            root(4)
            node_copies(TR_ATT, EV_ATT, hT, D)
            with act.Fori(0, TI) as i:
                for q in range(2):
                    hold(act, e_tr[2], i * 2 + (q + 1))
                    act.copy(onehot_t[:, 0:512], bank[0][:])
                    act.copy(onehot_t[:, 512:1024], bank[1][:]).then_inc(e_cp[2], 1)
            def copies(i, q):
                hold(act, e_tr[3], i * 2 + (q + 1))
                act.copy(onehot_t[:, 0:512], bank[0][:])
                act.copy(onehot_t[:, 512:1024], bank[1][:]).then_inc(e_cp[3], 1)

            def exps(i, q):
                hold(act, e_z[3], i * 2 + (q + 1))
                act.activation(ex[:], sc6[:], ACT.Exp).then_inc(e_fn[3], 1)

            run_ahead(act, copies, exps)
            node_copies(TR_TAIL, EV_TAIL, tail_t, TAIL)

        @block.tensor
        def _(pe):
            mm = nc.tensor.matmul
            pe.wait_ge(s_const, 7)
            for key in range(2):
                pe.wait_ge(v_l[2 * key], NH)
                mm(bank[0][:, 0:NH], tri[:], cnt[:], start=True, stop=True)
                mm(bank[1][:, 0:NH], ones[:], cnt[:], start=True, stop=True).then_inc(p_base, 1)
                pe.wait_ge(v_base, key + 1)
                for j in range(4):
                    last = mm(bank[2 + j][0:1, 0:TQ], not_first[0:NH, :], tile_ge[0:NH, j * TQ:(j + 1) * TQ],
                              start=True, stop=True)
                last.then_inc(p_hi, 1)

            for key in range(2):
                mm(bank[6][0:NH, 0:P], zero_bf[:, 0:NH], zero_bf[:, 0:P], start=True, stop=False)
                with pe.Fori(0, EI) as i:
                    for q in range(2):
                        g = i * 2 + (q + 2 * EI * key)
                        pe.wait_ge(v_oh, g + 1)
                        for u in range(U):
                            last = mm(bank[6][0:NH, 0:P], bh_hi[:, q, u, :], bh_lo[:, q, u, :],
                                      start=False, stop=False)
                        last.then_inc(p_hist, 1)
                mm(bank[6][0:NH, 0:P], zero_bf[:, 0:NH], zero_bf[:, 0:P], start=False, stop=True)\
                    .then_inc(p_hist_end, 1)
                pe.wait_ge(v_hist, key + 1)
                nc.tensor.transpose(bank[7][:, 0:NH], hist_sb[:], ident[0:NH, 0:NH]).then_inc(p_deg, 1)
            pe.wait_ge(s_w, 16 * W_LOADS)

            def transposes(tr, wait_h, src=h, width=D):
                def chunk(c):
                    c0_, n = CHUNKS[c]
                    if c == 0:
                        pe.wait_ge(v_h, wait_h)
                    if c >= 2:
                        pe.wait_ge(n_cp, NCH * tr + c - 1)
                    for j in range(n):
                        last = nc.tensor.transpose(bank[c % 2][0:width, j * P:(j + 1) * P], src[:, c0_ + j, :], ident[:])
                    last.then_inc(n_tr, 1)
                return chunk

            def project(ev, lhs, weights, width, tr=None, chunk=None):
                if chunk:
                    chunk(0)
                for c, (_, n) in enumerate(CHUNKS):
                    if chunk:
                        if c + 1 < NCH:
                            chunk(c + 1)
                        pe.wait_ge(n_cp, NCH * tr + c + 1)
                    if c >= 2:
                        pe.wait_ge(n_ev, NCH * ev + c - 1)
                    for j in range(n):
                        b, o = bank[2 + c % 2], j * width
                        if o + width > 512:
                            b, o = bank[4 + c % 2], 0
                        last = mm(b[:, o:o + width], lhs(c, j), weights, start=True, stop=True)
                    last.then_inc(n_mm, 1)

            def conv(k):
                with pe.Fori(0, TI) as i:
                    for q in range(2):
                        g = i * 2 + q
                        pe.wait_ge(e_oh[k], g + 1)
                        pe.wait_ge(d_gat[k][q], i * (16 * U) + 16 * U)
                        for u in range(U):
                            last = mm(bank[6 + q][:, u // 2 * D:(u // 2 + 1) * D], onehot[:, q, u, :], gat64[q][:, u, :],
                                      start=u % 2 == 0, stop=u % 2 == 1)
                        last.then_inc(e_out[k], 1)

            for k in range(5):
                project(k, lambda c, j: hT[:, c % 2, j * P:(j + 1) * P], w_conv[k][:], D,
                        tr=k, chunk=transposes(k, k + 1))
                conv(k)

            chunk = transposes(TR_L2, 6)
            for c in range(NCH):
                chunk(c)

            def layer_pe(j, m, src, ready, value):
                pe.wait_ge(ready, value)
                for c, (c0_, n) in enumerate(CHUNKS):
                    if c >= 2:
                        pe.wait_ge(f_act, NCH * j + c - 1)
                    mm(bank[2 + c % 2][0:D, 0:n * P], w_mlp[m][:], src[:, c0_ * P:(c0_ + n) * P],
                       start=True, stop=True).then_inc(f_mm, 1)

            def propagate(k):
                e = 5 + k

                def transposed(i, q):
                    pe.wait_ge(e_oh[e], i * 2 + (q + 1))
                    pe.wait_ge(d_pay[k][q], i * 16 + 16)
                    for u in range(U):
                        nc.tensor.transpose(bank[u // 4][:, u % 4 * P:(u % 4 + 1) * P], onehot[:, q, u, :], ident[:])
                        last = nc.tensor.transpose(bank[2 + u // 4][0:D, u % 4 * P:(u % 4 + 1) * P],
                                                   pay[:, q, u, 8:RW], ident[:])
                    last.then_inc(e_tr[k], 1)

                def products(i, q):
                    his = buckets(pe, 1, i, q)
                    pe.wait_ge(e_cp[k], i * 2 + (q + 1))
                    for u in range(U):
                        at = attr_t[:, u * P:(u + 1) * P]
                        mm(bank[5][:, u * D:(u + 1) * D], at, w_ew[:, D:2 * D], start=True, stop=True)
                        mm(bank[4][:, u * D:(u + 1) * D], at, w_ew[:, 0:D], start=True, stop=False)
                        last = mm(bank[4][:, u * D:(u + 1) * D], onehot_t[:, u * P:(u + 1) * P],
                                  hs_flat[:, bass.ds(his[u // 2] * D, D)], start=False, stop=True)
                    last.then_inc(e_mm[k], 1)

                def sums(i, q):
                    pe.wait_ge(e_msg[k], i * 2 + (q + 1))
                    for u in range(U):
                        last = mm(bank[6 + q][:, u // 2 * D:(u // 2 + 1) * D], onehot[:, q, u, :], msg[:, u, :],
                                  start=u % 2 == 0, stop=u % 2 == 1)
                    last.then_inc(e_out[e], 1)

                run_ahead(pe, transposed, products, sums)

            def ft(c, j):
                return FT[1][:, (c * CH + j) * P:(c * CH + j + 1) * P]

            layer_pe(0, "h", FT[0], n_cp, NCH * (TR_L2 + 1))
            pe.wait_ge(f_act, NCH)
            project(EV_PQ, ft, w_pq[:], 2 * D)
            propagate(0)
            chunk = transposes(TR_MEAN, 7)
            for c in range(NCH):
                chunk(c)
            layer_pe(1, "r1_1", FT[1], n_cp, NCH * (TR_MEAN + 1))
            layer_pe(2, "r1_2", FT[2], f_act, NCH * 2)
            layer_pe(3, "m", FT[1], f_res, NCH)
            layer_pe(4, "r2_1", FT[1], f_res, NCH * 2)
            layer_pe(5, "r2_2", FT[2], f_act, NCH * 5)
            layer_pe(6, "r3_1", FT[1], f_res, NCH * 3)
            layer_pe(7, "r3_2", FT[2], f_act, NCH * 7)
            pe.wait_ge(f_res, NCH * 4)
            project(EV_PQ + 1, ft, w_pq[:], 2 * D)
            for c, (c0_, n) in enumerate(CHUNKS):
                if c >= 2:
                    pe.wait_ge(n_cp, NCH * TR_BACK + c - 1)
                for j in range(n):
                    last = nc.tensor.transpose(bank[c % 2][:, j * D:(j + 1) * D], ft(c, j), ident[0:D, 0:D])
                last.then_inc(n_tr, 1)
            pe.wait_ge(n_cp, NCH * (TR_BACK + 1))
            propagate(1)

            project(EV_ATT, lambda c, j: hT[:, c % 2, j * P:(j + 1) * P], w_ha[:], PW,
                    tr=TR_ATT, chunk=transposes(TR_ATT, 8))

            def onehot_transposes(k, q):
                for u in range(U):
                    last = nc.tensor.transpose(bank[u // 4][:, u % 4 * P:(u % 4 + 1) * P], onehot[:, q, u, :], ident[:])
                last.then_inc(e_tr[k], 1)

            def look_up(k, i, q, table):
                his = buckets(pe, 1, i, q)
                pe.wait_ge(e_cp[k], i * 2 + (q + 1))
                for u in range(U):
                    last = mm(bank[7][:, u * HEADS:(u + 1) * HEADS], onehot_t[:, u * P:(u + 1) * P],
                              table[:, bass.ds(his[u // 2] * HEADS, HEADS)], start=True, stop=True)
                last.then_inc(e_mm[k], 1)

            def score_transposes(i, q):
                pe.wait_ge(e_oh[7], i * 2 + (q + 1))
                onehot_transposes(2, q)

            def masked_transposes(i, q):
                pe.wait_ge(e_msg[2], i * 2 + (q + 1))
                for u in range(U):
                    for hd in range(HEADS):
                        o = (2 * hd + u % 2) * P
                        last = nc.tensor.transpose(bank[2 + u // 2][:, o:o + P], masked[:, hd, u, :], ident[:])
                last.then_inc(e_out[7], 1)

            run_ahead(pe, score_transposes, lambda i, q: look_up(2, i, q, ai_tab), masked_transposes)

            def sum_transposes(i, q):
                pe.wait_ge(e_oh[8], i * 2 + (q + 1))
                onehot_transposes(3, q)

            def weighted_sums(i, q):
                pe.wait_ge(e_msg[3], i * 2 + (q + 1))
                for u in range(U):
                    o = u // 2 % 2 * LAS
                    last = mm(bank[2 + u // 4][:, o:o + LA], onehot[:, q, u, :], wrow[:, u, :],
                              start=u % 2 == 0, stop=u % 2 == 1)
                last.then_inc(e_out[8], 1)

            run_ahead(pe, sum_transposes, lambda i, q: look_up(3, i, q, smax), weighted_sums)
            tails = acc_a.rearrange("p (h w) -> p h w", w=LA)[:, :, HEADS * D:LA]
            project(EV_TAIL, lambda c, j: tail_t[:, c % 2, j * P:(j + 1) * P], w_tail[:], D,
                    tr=TR_TAIL, chunk=transposes(TR_TAIL, 9, src=tails, width=TAIL))

        @block.vector
        def _(dve):
            v = nc.vector
            do = Chain(dve, v_ch)

            def wide(ap, width):
                return ap.unsqueeze(2).to_broadcast([P, ap.shape[1], width])

            do(v.memset(tabs[0][:, :, 0], 0.0))
            v.memset(tabs[0][:, :, 1], PAD_LO).then_inc(s_fillable, 1)
            do(v.memset(tabs[1][:, TT:TX, 0], 0.0))
            do(v.memset(tabs[1][:, TT:TX, 1], PAD_LO))
            do(v.memset(pay[:], 0.0))
            v.memset(pay[:, :, :, 1], PAD_LO).then_inc(s_fillable, 1)
            do(v.memset(zero_bf[:], 0.0))
            do(v.memset(zeros_nh[:], 0.0))
            dve.wait_ge(s_const, 7)
            do(v.tensor_tensor(not_first[:], ones[:, 0:1], ident[:, 0:1], ALU.subtract))
            dve.wait_ge(s_key, 32)

            for key in range(2):
                do(v.tensor_scalar(mask, key_i[key], 7, None, ALU.arith_shift_right))
                do(v.tensor_copy(hi_f[key], mask))
                do(v.tensor_scalar(mask, key_i[key], P - 1, None, ALU.bitwise_and))
                do(v.tensor_copy(lo_f[key], mask))
                do(v.tensor_copy(key_f[key], key_i[key]))

            def rank(key):
                steps = Chain(dve, v_l[2 * key])
                with dve.Fori(0, NH) as b:
                    steps.base, steps.n = b, 0
                    steps(v.tensor_scalar(scan, hi_f[key], iota_hi[:, bass.ds(b, 1)], 0.0, ALU.is_equal, ALU.add,
                                          accum_out=cnt[:, bass.ds(b, 1)]))
                dve.wait_ge(p_base, key + 1)
                before, total = bank[0][:, 0:NH], bank[1][:, 0:NH]
                do(v.tensor_scalar(tiles_f[:], total, float(PAIR - 1), None, ALU.add))
                do(v.tensor_copy(tiles_i[:], tiles_f[:]))
                do(v.tensor_scalar(tiles_i[:], tiles_i[:], 8, None, ALU.arith_shift_right))
                do(v.tensor_scalar(tiles_f[:], tiles_i[:], 2.0, None, ALU.mult))
                do(v.tensor_tensor_scan(tiles_inc[:], tiles_f[:], zeros_nh[:], 0.0, ALU.add, ALU.add))
                do(v.tensor_tensor(first_tile[:], tiles_inc[:], tiles_f[:], ALU.subtract))
                do(v.scalar_tensor_tensor(start[:], first_tile[:], float(P), before, ALU.mult, ALU.add))
                do(v.tensor_scalar(start[:], start[:], -1.0, None, ALU.add))
                do(v.tensor_tensor(diag[0:NH, :], first_tile[0:NH, :], ident[0:NH, 0:NH], ALU.mult))
                do(v.tensor_reduce(bcol[0:NH, :], diag[0:NH, :], AX.X, ALU.add))
                v.tensor_scalar(tile_ge[0:NH, :], tile_iota[0:NH, :], bcol[0:NH, 0:1], None, ALU.is_ge)\
                    .then_inc(v_base, 1)
                dve.wait_ge(p_hi, key + 1)
                for j in range(4):
                    do(v.tensor_copy(hi_scratch[:, j * TQ:(j + 1) * TQ], bank[2 + j][0:1, 0:TQ]))
                by_group = hi_scratch.rearrange("o (g u) -> o g u", u=U)
                word = by_group[:, :, U - 1]
                for p in range(PAIRS - 2, -1, -1):
                    do(v.scalar_tensor_tensor(word, word, float(1 << HI_BITS), by_group[:, :, 2 * p], ALU.mult, ALU.add))
                do(v.tensor_copy(hi_row[key][:], word))
                do(v.memset(zeros, 0.0))
                do(v.memset(pos_f, float(P * P * TT)))
                steps = Chain(dve, v_l[2 * key + 1])
                with dve.Fori(0, NH) as b:
                    steps.base, steps.n = b * 3, 0
                    steps(v.tensor_scalar(mask, hi_f[key], iota_hi[:, bass.ds(b, 1)], None, ALU.is_equal))
                    steps(v.tensor_tensor_scan(scan, mask, zeros, start[:, bass.ds(b, 1)], ALU.add, ALU.add))
                    dve.sem_inc(s_passed, 1)
                    steps(v.copy_predicated(pos_f, mask, scan))
                do(v.tensor_copy(mask, pos_f))
                do(v.tensor_scalar(scan.bitcast(I32), mask, P - 1, None, ALU.bitwise_and))
                do(v.tensor_scalar(mask, mask, 7, None, ALU.arith_shift_right))
                v.scalar_tensor_tensor(pos_i[key], scan.bitcast(I32), float(TT), mask, ALU.mult, ALU.add)\
                    .then_inc(v_pos, 1)

            rank(0)
            dve.wait_ge(v_pos, 1)
            rank(1)

            def histogram(key):
                base = 2 * EI * key

                def group(i, q):
                    cols = bass.ds(i * (2 * U) + q * U, U)
                    v.tensor_tensor(bh_hi[:, q], iota_hi[:].unsqueeze(1).to_broadcast([P, U, NH]),
                                    wide(hi_f[key][:, cols], NH), ALU.is_equal)
                    v.tensor_tensor(bh_lo[:, q], iota_lo[:].unsqueeze(1).to_broadcast([P, U, P]),
                                    wide(lo_f[key][:, cols], P), ALU.is_equal).then_inc(v_oh, 1)

                for q in range(2):
                    if base:
                        dve.wait_ge(p_hist, base + q - 1)
                    group(0, q)
                with dve.Fori(1, EI) as i:
                    for q in range(2):
                        dve.wait_ge(p_hist, i * 2 + (base + q - 1))
                        group(i, q)
                dve.wait_ge(p_hist_end, key + 1)
                v.tensor_copy(hist_sb[:], bank[6][0:NH, 0:P]).then_inc(v_hist, 1)
                dve.wait_ge(p_deg, key + 1)
                do(v.tensor_copy(degree[key][:], bank[7][:, 0:NH]))

            histogram(0)
            histogram(1)
            v.tensor_scalar(stat2[:], degree[0][:], 1.0, None, ALU.add).then_inc(dve_ln, 1)
            do(v.tensor_scalar(mean_w[:], degree[1][:], 1.0, None, ALU.max))
            do(v.reciprocal(mean_w[:], mean_w[:]))
            dve.wait_ge(act_ln, 1)
            do(v.reciprocal(dinv[:], stat[:]))

            def norm_relu(n):
                do(v.tensor_reduce(stat[:], x[:], AX.X, ALU.add))
                do(v.tensor_scalar(stat[:], stat[:], 1.0 / D, None, ALU.mult))
                do(v.tensor_tensor(h[:], x[:], wide(stat[:], D), ALU.subtract))
                do(v.tensor_tensor(acc[:], h[:], h[:], ALU.mult))
                do(v.tensor_reduce(stat2[:], acc[:], AX.X, ALU.add))
                v.tensor_scalar(stat2[:], stat2[:], 1.0 / D, LN_EPS, ALU.mult, ALU.add).then_inc(dve_ln, 1)
                dve.wait_ge(act_ln, n + 2)
                do(v.reciprocal(stat2[:], stat[:]))
                do(v.tensor_tensor(h[:], h[:], wide(stat2[:], D), ALU.mult))
                v.tensor_scalar(h[:], h[:], 0.0, None, ALU.max).then_inc(v_h, 1)

            def feed_indices(k, t, i, q):
                g = i * (2 * U) + q * U
                v.tensor_copy(ring_i[:, q, :], tabs[t][:, bass.ds(g, U), 0]).then_inc(e_idx[k], 1)

            def feed_onehot(k, t, i, q):
                g = i * (2 * U) + q * U
                v.tensor_tensor(onehot[:, q], iota_lo[:].unsqueeze(1).to_broadcast([P, U, P]),
                                wide(tabs[t][:, bass.ds(g, U), 1], P), ALU.is_equal).then_inc(e_oh[k], 1)

            def edge_pass(k, t, sums, width, product=None):
                for q in range(2):
                    feed_indices(k, t, 0, q)
                    feed_onehot(k, t, 0, q)
                adds = Chain(dve, e_add[k])
                with dve.Fori(0, TI) as i:
                    adds.base, adds.n = i * (2 * PAIRS), 0
                    for q in range(2):
                        if product:
                            product(i, q)
                        his = buckets(dve, t, i, q)
                        dve.wait_ge(e_out[k], i * 2 + (q + 1))
                        dve.sem_inc(s_passed, 1)
                        feed_indices(k, t, i + 1, q)
                        for p in range(PAIRS):
                            o = sums[0][:, bass.ds(his[p] * width, width)]
                            adds(v.tensor_tensor(o, o, sums[1](q, p), ALU.add))
                        feed_onehot(k, t, i + 1, q)

            psum_rows = lambda q, p: bank[6 + q][:, p * D:(p + 1) * D]

            dve.wait_ge(s_w, 16 * W_LOADS)
            for part in range(2):
                o = HEADS * D + part * HEADS
                for rows, tile in ((D, w_ha), (P, b_ha)):
                    both = acc_flat[0:rows, 0:HEADS * D].rearrange("p (h d) -> p h d", h=HEADS)
                    do(v.tensor_tensor(both, tile[:, 0:HEADS * D].rearrange("p (h d) -> p h d", h=HEADS),
                                       att_bc[0:rows, :, part, :], ALU.mult))
                    do(v.tensor_reduce(tile[:, o:o + HEADS], both, AX.X, ALU.add))
            both = acc_flat[:, 0:HEADS * D].rearrange("p (h d) -> p h d", h=HEADS)
            do(v.tensor_tensor(both, be5_bc, att_bc[:, :, 1, :], ALU.mult))
            do(v.tensor_reduce(c0[:], both, AX.X, ALU.add))
            aj = b_ha[:, HEADS * D + HEADS:PW]
            do(v.tensor_tensor(aj, aj, c0[:], ALU.add))
            for f in range(NB5):
                do(v.tensor_tensor(both, we5_bc[:, f], att_bc[:, :, 1, :], ALU.mult))
                do(v.tensor_reduce(w5[:, :, f], both, AX.X, ALU.add))
            dve.wait_ge(s_x, 32)
            norm_relu(0)
            for k in range(5):
                if k:
                    dve.wait_ge(d_table, 16 * k)
                for c, (c0_, n) in enumerate(CHUNKS):
                    dve.wait_ge(n_mm, NCH * k + c + 1)
                    v.tensor_tensor(hs[:, c0_:c0_ + n, :],
                                    bank[2 + c % 2][:, 0:n * D].rearrange("p (h d) -> p h d", d=D),
                                    wide(dinv[:, c0_:c0_ + n], D), ALU.mult).then_inc(n_ev, 1)
                do(v.memset(acc[:], 0.0))
                if k == 0:
                    dve.wait_ge(d_tab, 32)
                edge_pass(k, 0, (acc_flat, psum_rows), D)
                dve.wait_ge(n_ev, NCH * (k + 1))
                do(v.tensor_tensor(acc[:], acc[:], hs[:], ALU.add))
                do(v.tensor_tensor(acc[:], acc[:], wide(dinv[:], D), ALU.mult))
                do(v.tensor_tensor(acc[:], acc[:], b_conv[k][:].unsqueeze(1).to_broadcast([P, NH, D]), ALU.add))
                if k in (2, 4):
                    do(v.tensor_tensor(x[:], x[:], acc[:], ALU.add))
                    norm_relu(1 if k == 2 else 2)
                else:
                    v.tensor_scalar(h[:], acc[:], 0.0, None, ALU.max).then_inc(v_h, 1)

            def propagate(k):
                dve.wait_ge(d_table, 16 * (5 + k))
                for c, (c0_, n) in enumerate(CHUNKS):
                    dve.wait_ge(n_mm, NCH * (EV_PQ + k) + c + 1)
                    pq = bank[2 + c % 2][:, 0:n * 2 * D].rearrange("p (h d) -> p h d", d=2 * D)
                    do(v.tensor_tensor(hs[:, c0_:c0_ + n, :], pq[:, :, 0:D],
                                       be_bc[:].unsqueeze(1).to_broadcast([P, n, D]), ALU.add))
                    v.tensor_copy(acc[:, c0_:c0_ + n, :], pq[:, :, D:2 * D]).then_inc(n_ev, 1)
                if k == 1:
                    for c, (c0_, n) in enumerate(CHUNKS):
                        dve.wait_ge(n_tr, NCH * TR_BACK + c + 1)
                        xs = x[:, c0_:c0_ + n, :]
                        v.tensor_tensor(xs, xs, bank[c % 2][:, 0:n * D].rearrange("p (h d) -> p h d", d=D), ALU.add)\
                            .then_inc(n_cp, 1)
                dve.wait_ge(d_table, 16 * (6 + k))
                do(v.memset(acc[:], 0.0))

                def product(i, q):
                    g = i * 2 + q
                    dve.wait_ge(d_gat[5 + k][q], i * (16 * U) + 16 * U)
                    dve.wait_ge(e_mm[k], g + 1)
                    v.tensor_tensor(zed, bank[4][:].rearrange("p (u d) -> p u d", d=D), gat64[q], ALU.add)\
                        .then_inc(e_z[k], 1)
                    dve.wait_ge(e_fn[k], g + 1)
                    v.tensor_tensor(msg, msg, bank[5][:].rearrange("p (u d) -> p u d", d=D), ALU.mult)\
                        .then_inc(e_msg[k], 1)

                edge_pass(5 + k, 1, (acc_flat, psum_rows), D, product)

            def residual(j, n, other):
                for c, (c0_, m) in enumerate(CHUNKS):
                    dve.wait_ge(f_act, NCH * j + c + 1)
                    cols = slice(c0_ * P, (c0_ + m) * P)
                    v.tensor_tensor(FT[1][:, cols], FT[1][:, cols], other[:, cols], ALU.add).then_inc(f_res, 1)

            propagate(0)
            v.tensor_tensor(h[:], acc[:], wide(mean_w[:], D), ALU.mult).then_inc(v_h, 1)
            for c, (c0_, n) in enumerate(CHUNKS):
                dve.wait_ge(n_tr, NCH * TR_MEAN + c + 1)
                cols = slice(c0_ * P, (c0_ + n) * P)
                v.tensor_tensor(FT[1][:, cols], FT[1][:, cols], bank[c % 2][0:D, 0:n * P], ALU.add).then_inc(n_cp, 1)
            residual(2, 0, FT[2])
            residual(3, 1, FT[0])
            residual(5, 2, FT[2])
            residual(7, 3, FT[2])
            propagate(1)
            do(v.tensor_tensor(acc[:], acc[:], wide(mean_w[:], D), ALU.mult))
            dve.wait_ge(n_cp, NCH * (TR_BACK + 1))
            do(v.tensor_tensor(x[:], x[:], acc[:], ALU.add))

            norm_relu(3)
            for c, (c0_, n) in enumerate(CHUNKS):
                dve.wait_ge(n_mm, NCH * EV_ATT + c + 1)
                m = min(n, 3)
                last = v.tensor_tensor(proj[:, c0_:c0_ + m, :],
                                       bank[2 + c % 2][:, 0:m * PW].rearrange("p (h d) -> p h d", d=PW),
                                       b_ha[:].unsqueeze(1).to_broadcast([P, m, PW]), ALU.add)
                if n > 3:
                    do(last)
                    last = v.tensor_tensor(proj[:, c0_ + 3, :], bank[4 + c % 2][:, 0:PW], b_ha[:], ALU.add)
                last.then_inc(n_ev, 1)
            dve.wait_ge(n_ev, NCH * (EV_ATT + 1))
            do(v.tensor_copy(ai_tab.rearrange("p (h t) -> p h t", t=HEADS), proj[:, :, HEADS * D:HEADS * D + HEADS]))
            do(v.memset(smax, -BIG))

            SC = 8
            for q in range(2):
                feed_indices(7, 1, 0, q)
                feed_onehot(7, 1, 0, q)
            adds, steps = Chain(dve, e_add[7]), Chain(dve, e_v[0])
            with dve.Fori(0, TI) as i:
                adds.base, adds.n = i * (2 * PAIRS), 0
                steps.base, steps.n = i * (2 * SC), 0
                for q in range(2):
                    g = i * 2 + q
                    dve.wait_ge(d_pay[2][q], i * 16 + 16)
                    v5 = pay[:, q, :, 2:2 + NB5].unsqueeze(2).to_broadcast([P, U, HEADS, NB5])
                    steps(v.tensor_tensor(prod5[:], v5, w5[:].unsqueeze(1).to_broadcast([P, U, HEADS, NB5]), ALU.mult))
                    steps(v.tensor_reduce(sc5[:], prod5[:], AX.X, ALU.add))
                    dve.wait_ge(d_gat[7][q], i * (16 * U) + 16 * U)
                    steps(v.tensor_tensor(sc5[:], sc5[:], gat2[q], ALU.add))
                    dve.wait_ge(e_mm[2], g + 1)
                    steps(v.tensor_tensor(sc5[:], sc5[:], bank[7][:, 0:U * HEADS].rearrange("p (u h) -> p u h", h=HEADS), ALU.add))
                    steps(v.scalar_tensor_tensor(sc6[:], sc5[:], SLOPE, sc5[:], ALU.mult, ALU.max))
                    steps(v.tensor_copy(alpha_all[:, bass.ds(g * (U * HEADS), U * HEADS)],
                                        sc6[:].rearrange("p u h -> p (u h)")))
                    steps(v.tensor_scalar(penalty, onehot[:, q], BIG, -BIG, ALU.mult, ALU.add))
                    steps(v.tensor_tensor(masked[:, 0], penalty, wide(sc6[:, :, 0], P), ALU.add))
                    v.tensor_tensor(masked[:, 1], penalty, wide(sc6[:, :, 1], P), ALU.add).then_inc(e_msg[2], 1)
                    dve.wait_ge(e_msg[2], g + 1)
                    dve.sem_inc(s_passed, 1)
                    feed_indices(7, 1, i + 1, q)
                    feed_onehot(7, 1, i + 1, q)
                    his = buckets(dve, 1, i, q)
                    dve.wait_ge(e_out[7], g + 1)
                    for b in range(PAIRS):
                        last = v.tensor_reduce(tmax[:, b, :],
                                               bank[2 + b][:].rearrange("p (n e) -> p n e", e=PAIR), AX.X, ALU.max)
                    last.then_inc(e_z[2], 1)
                    dve.wait_ge(e_z[2], g + 1)
                    for p in range(PAIRS):
                        o = smax[:, bass.ds(his[p] * HEADS, HEADS)]
                        adds(v.tensor_tensor(o, o, tmax[:, p, :], ALU.max))
                assert steps.n == 2 * SC and adds.n == 2 * PAIRS

            do(v.memset(acc_a, 0.0))

            ST = 3

            def weigh(i, q):
                g = i * 2 + q
                if q == 0:
                    steps.base, steps.n = i * (2 * ST), 0
                dve.wait_ge(e_mm[3], g + 1)
                steps(v.tensor_tensor(sc5[:].rearrange("p u h -> p (u h)"),
                                      alpha_all[:, bass.ds(g * (U * HEADS), U * HEADS)],
                                      bank[7][:, 0:U * HEADS], ALU.subtract))
                v.tensor_scalar(sc6[:], sc5[:], 0.0, None, ALU.min).then_inc(e_z[3], 1)
                dve.wait_ge(d_gat[8][q], i * (16 * U) + 16 * U)
                dve.wait_ge(d_pay[3][q], i * 16 + 16)
                dve.wait_ge(e_fn[3], g + 1)
                steps(v.tensor_tensor(wrow[:, :, 0:HEADS * D].rearrange("p u (h d) -> p u h d", h=HEADS),
                                      gat[:, q].rearrange("p u (h d) -> p u h d", h=HEADS),
                                      ex[:].unsqueeze(3).to_broadcast([P, U, HEADS, D]), ALU.mult))
                steps(v.tensor_tensor(wrow[:, :, HEADS * D:HEADS * (D + NB5)].rearrange("p u (h f) -> p u h f", h=HEADS),
                                      pay[:, q, :, 2:2 + NB5].unsqueeze(2).to_broadcast([P, U, HEADS, NB5]),
                                      ex[:].unsqueeze(3).to_broadcast([P, U, HEADS, NB5]), ALU.mult))
                v.tensor_copy(wrow[:, :, HEADS * (D + NB5):LA], ex[:]).then_inc(e_msg[3], 1)

            steps = Chain(dve, e_v[1])
            edge_pass(8, 1, (acc_a, lambda q, p: bank[2 + p // 2][:, p % 2 * LAS:p % 2 * LAS + LA]), LA, weigh)

            sums = acc_a.rearrange("p (h w) -> p h w", w=LA)
            do(v.tensor_scalar(rden[:], sums[:, :, HEADS * (D + NB5):LA], 1e-16, None, ALU.add))
            do(v.reciprocal(rden[:], rden[:]))
            do(v.tensor_scalar(rden[:], rden[:], 1.0 / HEADS, None, ALU.mult))
            for hd in range(HEADS):
                r = rden[:, :, hd]
                do(v.tensor_tensor(hs[:], sums[:, :, hd * D:(hd + 1) * D], wide(r, D), ALU.mult))
                do(v.tensor_tensor(x[:], x[:], hs[:], ALU.add))
                t = sums[:, :, HEADS * D + hd * NB5:HEADS * D + (hd + 1) * NB5]
                do(v.tensor_tensor(t, t, wide(r, NB5), ALU.mult))
            t = sums[:, :, HEADS * (D + NB5):LA]
            v.tensor_tensor(t, t, rden[:], ALU.mult).then_inc(v_h, 1)
            for c, (c0_, n) in enumerate(CHUNKS):
                dve.wait_ge(n_mm, NCH * EV_TAIL + c + 1)
                xs = x[:, c0_:c0_ + n, :]
                v.tensor_tensor(xs, xs, bank[2 + c % 2][:, 0:n * D].rearrange("p (h d) -> p h d", d=D), ALU.add)\
                    .then_inc(n_ev, 1)
            dve.wait_ge(n_ev, NCH * (EV_TAIL + 1))
            v.tensor_tensor(x[:], x[:], bias_bc[:].unsqueeze(1).to_broadcast([P, NH, D]), ALU.add).then_inc(v_h, 1)


def kernel(**inputs):
    import numpy as np
    from concourse import bacc
    from concourse.bass_utils import run_bass_kernel_spmd

    nc = bacc.Bacc("TRN2", target_bir_lowering=False, num_devices=1)
    arrays, aps = {}, {}
    for name, value in inputs.items():
        v = np.ascontiguousarray(value)
        if name == "edge_weight":
            continue
        if name in ("src", "dst"):
            v = np.concatenate([v, np.full((EP - E,), NP, v.dtype)])
        elif name in ("edge_attr_5", "edge_attr_64"):
            v = np.concatenate([v, np.zeros((EP - E, v.shape[1]), v.dtype)])
        arrays["in_" + name] = v
        aps[name] = nc.dram_tensor("in_" + name, v.shape, mybir.dt.from_np(v.dtype), kind="ExternalInput").ap()
    out = nc.dram_tensor("out", (N, D), F32, kind="ExternalOutput").ap()
    build(nc, aps, out)
    return run_bass_kernel_spmd(nc, [arrays], core_ids=[0]).results[0]["out"]
```
